# Optimizing a Trainium2 kernel written in Bass

```python
import numpy as np
import jax
import jax.numpy as jnp

def _softmax(x, axis=-1):
    return jax.nn.softmax(x, axis=axis)

def _gelu(x):
    return jax.nn.gelu(x, approximate=True)

def _silu(x):
    return jax.nn.silu(x)

def _sigmoid(x):
    return jax.nn.sigmoid(x)

def _layernorm(x, axis=-1, eps=1e-05):
    m = jnp.mean(x, axis=axis, keepdims=True)
    v = jnp.var(x, axis=axis, keepdims=True)
    return (x - m) / jnp.sqrt(v + eps)

def _scatter_add(tgt, idx, src, axis=0):
    return tgt.at[idx].add(src)

def _segment_sum(src, seg, n):
    return jax.ops.segment_sum(src, seg, n)
kernel_name = 'mk_cond_resid_d1_seqx_r2_26c2ff'

def setup_inputs(seed: int=0):
    np.random.seed(seed)
    _w = jnp.asarray

    def _rec_inputs():
        import jax
        import jax.numpy as jnp
        _rk = jax.random.key(seed)
        x = -0.000125 + 0.9999 * jax.random.normal(jax.random.fold_in(_rk, 1), (32, 512, 512), jnp.float32)
        _lenS = 512 - jax.random.randint(jax.random.fold_in(_rk, 7), (32,), 0, max(1, 512 // 4) + 1, jnp.int32)
        _lenS2 = 512 - jax.random.randint(jax.random.fold_in(_rk, 8), (32,), 0, max(1, 512 // 4) + 1, jnp.int32)
        cond_1024 = -0.00493535 + 1.00056 * jax.random.normal(jax.random.fold_in(_rk, 11), (32, 512), jnp.float32)
        return (x, cond_1024)
    x, cond_1024 = _rec_inputs()

    def _L0_cond_setup():
        import jax, jax.numpy as jnp
        import numpy as np
        import math
        N, T, D, H = (64, 256, 512, 512)

        def lstm_forward(x, h0, Wx, Wh, b):
            Hd = h0.shape[1]
            xW = jnp.einsum('ntd,dg->ntg', x, Wx) + b
            c0 = jnp.zeros_like(h0)

            def step(carry, xw_t):
                prev_h, prev_c = carry
                a = xw_t + prev_h @ Wh
                i = jax.nn.sigmoid(a[:, :Hd])
                f = jax.nn.sigmoid(a[:, Hd:2 * Hd])
                o = jax.nn.sigmoid(a[:, 2 * Hd:3 * Hd])
                g = jnp.tanh(a[:, 3 * Hd:])
                next_c = f * prev_c + i * g
                next_h = o * jnp.tanh(next_c)
                return ((next_h, next_c), next_h)
            (_, _), hs = jax.lax.scan(step, (h0, c0), jnp.swapaxes(xW, 0, 1))
            return jnp.swapaxes(hs, 0, 1)
        key = jax.random.key(seed)
        k1, k2, k3, k4 = jax.random.split(key, 4)
        x = jax.random.normal(k1, (N, T, D), dtype=jnp.float32)
        h0 = jax.random.normal(k2, (N, H), dtype=jnp.float32)
        Wx = jax.random.normal(k3, (D, 4 * H), dtype=jnp.float32) / math.sqrt(D)
        Wh = jax.random.normal(k4, (H, 4 * H), dtype=jnp.float32) / math.sqrt(H)
        b = jnp.zeros((4 * H,), dtype=jnp.float32)
        return {'x': x, 'h0': h0, 'Wx': Wx, 'Wh': Wh, 'b': b}
    _L0_cond_all = _L0_cond_setup()
    _L0_cond_in = {k: v for k, v in _L0_cond_all.items() if k in ('Wx', 'Wh', 'b')}
    del _L0_cond_all
    return {'x': x, 'cond_1024': cond_1024, 'L0_cond_Wx': _L0_cond_in['Wx'], 'L0_cond_Wh': _L0_cond_in['Wh'], 'L0_cond_b': _L0_cond_in['b']}

def reference(x, cond_1024, L0_cond_Wx, L0_cond_Wh, L0_cond_b):
    import jax
    import jax.numpy as jnp

    def _L0_cond_ref(x, h0, Wx, Wh, b):
        import jax, jax.numpy as jnp
        import numpy as np
        import math
        N, T, D, H = (64, 256, 512, 512)

        def lstm_forward(x, h0, Wx, Wh, b):
            Hd = h0.shape[1]
            xW = jnp.einsum('ntd,dg->ntg', x, Wx) + b
            c0 = jnp.zeros_like(h0)

            def step(carry, xw_t):
                prev_h, prev_c = carry
                a = xw_t + prev_h @ Wh
                i = jax.nn.sigmoid(a[:, :Hd])
                f = jax.nn.sigmoid(a[:, Hd:2 * Hd])
                o = jax.nn.sigmoid(a[:, 2 * Hd:3 * Hd])
                g = jnp.tanh(a[:, 3 * Hd:])
                next_c = f * prev_c + i * g
                next_h = o * jnp.tanh(next_c)
                return ((next_h, next_c), next_h)
            (_, _), hs = jax.lax.scan(step, (h0, c0), jnp.swapaxes(xW, 0, 1))
            return jnp.swapaxes(hs, 0, 1)
        return lstm_forward(x, h0, Wx, Wh, b)
    x = x + _L0_cond_ref(x, cond_1024, L0_cond_Wx, L0_cond_Wh, L0_cond_b)
    return x

_drawn_inputs = setup_inputs


def setup_inputs(seed=0):
    import zlib

    import numpy as np

    out = dict(_drawn_inputs(seed))
    spreads = {'L0_cond_b': (0.0, 0.1)}
    factors = {}
    for name, (base, spread) in spreads.items():
        noise = np.random.default_rng([zlib.crc32(name.encode()), seed]).standard_normal(out[name].shape)
        drawn = base * np.exp(spread * noise) if base else spread * noise
        out[name] = jnp.asarray(drawn.astype(out[name].dtype))
    for name, factor in factors.items():
        out[name] = (out[name] * factor).astype(out[name].dtype)
    return out
```

```python
from contextlib import ExitStack

import numpy as np
import concourse.bass as bass
from concourse import mybir

F32 = mybir.dt.float32
F32R = mybir.dt.float32r
F16 = mybir.dt.float16
I32 = mybir.dt.int32
ALU = mybir.AluOpType
ACT = mybir.ActivationFunctionType
AX = mybir.AxisListType


def lstm_residual(nc, x, h0, Wx, Wh, bias, out):
    B, T, D = x.shape
    H = h0.shape[1]
    G = 4 * H
    P = 128
    NJ = H // P
    C = P
    NCH = D // P
    L = 32
    ZW = 4 * C
    TB = P // B
    NB = T // TB
    BODY = 2
    LEAD = 2
    H_SCALE = 4096.0
    H_SCALE_LOG2 = 12
    EXP_ONE = 127
    W_TOP = 14
    MIN_FIELD = W_TOP + H_SCALE_LOG2 + 1
    MANT = 23

    ctx = ExitStack()
    with ctx:
        def sb(name, shape, dt=F32):
            return ctx.enter_context(nc.sbuf_tensor(name, shape, dt))

        def bank(name):
            return ctx.enter_context(nc.psum_tensor(name, [P, 512], F32))

        def sem(name):
            return ctx.enter_context(nc.semaphore(name))

        wx_hi = sb("wx_hi", [P, NCH, G], F32R)
        wx_lo = sb("wx_lo", [P, NCH, G], F32R)
        wh_hi = sb("wh_hi", [P, NCH, G], F16)
        wh_lo = sb("wh_lo", [P, NCH, G], F16)
        shared = sb("shared", [P, 4 * G])
        wh_raw = shared[:, :].rearrange("p (ch g) -> p ch g", ch=NCH)
        stage = shared[:, 0:2 * G].rearrange("p (r j n) -> p r j n", r=2, j=NJ)
        xw = shared[:, 2 * G:4 * G].rearrange("p (r t n) -> p r t n", r=2, t=TB)
        wx_raw = sb("wx_raw", [P, 2, G])
        bias_bc = sb("bias_bc", [P, G])
        x_in = sb("x_in", [P, 2, TB, C])
        x_T = sb("x_T", [P, NCH, TB, B])
        x_hi = sb("x_hi", [P, 2, NCH, TB * B], F32R)
        x_lo = sb("x_lo", [P, 2, NCH, TB * B], F32R)
        x_res = sb("x_res", [P, 2, TB, C])
        y = sb("y", [P, 2, TB, C])
        h0_in = sb("h0_in", [P, C])
        h0_T = sb("h0_T", [P, NCH, B])
        zx = sb("zx", [P, ZW])
        act = sb("act", [P, ZW])
        fc = sb("fc", [P, C])
        ig = sb("ig", [P, C])
        c = sb("c", [P, C])
        tanh_c = sb("tanh_c", [P, C])
        h32 = sb("h32", [P, 2, C])
        h_hi = sb("h_hi", [P, C], F16)
        h_lo = sb("h_lo", [P, C], F16)
        hT_hi = sb("hT_hi", [P, NCH, B], F16)
        hT_lo = sb("hT_lo", [P, NCH, B], F16)
        wmax4 = sb("wmax4", [P, NCH])
        wmax = sb("wmax", [P, 1])
        wmax_all = sb("wmax_all", [P, 1])
        field = sb("field", [P, 1], I32)
        field2 = sb("field2", [P, 1], I32)
        w_scale = sb("w_scale", [P, 1], I32)
        z_scale = sb("z_scale", [P, 1], I32)

        Z = bank("Z")
        PS = [bank("PS0"), bank("PS1")]

        wx_loaded = [sem("wx_loaded0"), sem("wx_loaded1")]
        wh_loaded = [sem(f"wh_loaded{ch}") for ch in range(NCH)]
        bias_loaded = sem("bias_loaded")
        h0_loaded = sem("h0_loaded")
        x_loaded = [sem("x_loaded0"), sem("x_loaded1")]
        res_loaded = [sem("res_loaded0"), sem("res_loaded1")]
        xw_placed = [sem("xw_placed0"), sem("xw_placed1")]
        y_stored = [sem("y_stored0"), sem("y_stored1")]
        wx_hi_cut = sem("wx_hi_cut")
        wx_lo_cut = sem("wx_lo_cut")
        wmax4_done = sem("wmax4_done")
        wmax_done = sem("wmax_done")
        wmax_shared = sem("wmax_shared")
        scale_step = sem("scale_step")
        scales_done = sem("scales_done")
        wh_hi_cut = sem("wh_hi_cut")
        wh_lo_cut = sem("wh_lo_cut")
        h0_turned = sem("h0_turned")
        c_cleared = sem("c_cleared")
        x_turned = sem("x_turned")
        x_hi_cut = sem("x_hi_cut")
        x_lo_cut = sem("x_lo_cut")
        proj_done = sem("proj_done")
        proj_staged = sem("proj_staged")
        z_done = sem("z_done")
        zx_if_done = sem("zx_if_done")
        zx_g_done = sem("zx_g_done")
        zx_o_done = sem("zx_o_done")
        sig_if_done = sem("sig_if_done")
        tanh_g_done = sem("tanh_g_done")
        sig_o_done = sem("sig_o_done")
        fc_done = sem("fc_done")
        ig_done = sem("ig_done")
        c_done = sem("c_done")
        tanh_c_done = sem("tanh_c_done")
        h_hi_done = sem("h_hi_done")
        hT_hi_done = sem("hT_hi_done")
        h32_done = sem("h32_done")
        h_lo_done = sem("h_lo_done")
        hT_lo_done = sem("hT_lo_done")
        y_done = sem("y_done")

        x_view = x.rearrange("b t (j c) -> j b t c", j=NJ)
        out_view = out.rearrange("b t (j c) -> j b t c", j=NJ)
        wx_view = Wx.rearrange("(j ch l) g -> ch j l g", j=NJ, ch=NCH)
        wh_view = Wh.rearrange("(j ch l) g -> ch j l g", j=NJ, ch=NCH)
        h0_view = h0.rearrange("b (j c) -> j b c", j=NJ)

        I, F, O, Gt = (slice(g * C, (g + 1) * C) for g in range(4))
        IF = slice(0, 2 * C)

        def by_tile(w):
            return w.rearrange("p (g j c) -> p j g c", g=4, j=NJ)

        def as_tiles(w):
            return w.rearrange("p (j g c) -> p j g c", g=4, j=NJ)

        def started(value):
            return not isinstance(value, int) or value > 0

        def run_blocks(engine, block):
            def body(i, static):
                for r in range(BODY):
                    n = i * BODY + r
                    block(i, n, r, (lambda k, n=n: n + k < NB) if static else (lambda k: True))
            last = NB // BODY
            body(0, True)
            with engine.Fori(1, last - 2) as i:
                body(i, False)
            body(last - 2, True)
            body(last - 1, True)

        block_ctx = ctx.enter_context(nc.Block())

        @block_ctx.sync
        def _(sp):
            def load_x(n, r):
                for j in range(NJ):
                    sp.dma_start(x_in[L * j:L * j + B, r], x_view[j, :, bass.ds(n * TB, TB), :]).then_inc(x_loaded[r], 16)

            def load_res(n, r):
                for j in range(NJ):
                    sp.dma_start(x_res[L * j:L * j + B, r], x_view[j, :, bass.ds(n * TB, TB), :]).then_inc(res_loaded[r], 16)

            def place_xw(r):
                for t in range(TB):
                    for j in range(NJ):
                        sp.dma_start(xw[L * j:L * j + B, r, t], stage[B * t:B * t + B, r, j]).then_inc(xw_placed[r], 16)

            for j in range(NJ):
                sp.dma_start(h0_in[L * j:L * j + B], h0_view[j]).then_inc(h0_loaded, 16)
            for ch in range(NCH):
                for j in range(NJ):
                    sp.dma_start(wh_raw[L * j:L * j + L, ch], wh_view[ch, j]).then_inc(wh_loaded[ch], 16)
                if ch < 2:
                    for j in range(NJ):
                        sp.dma_start(wx_raw[L * j:L * j + L, ch], wx_view[ch, j]).then_inc(wx_loaded[ch], 16)
            load_x(0, 0)
            load_x(1, 1)
            sp.dma_start(bias_bc[:, :], bias.partition_broadcast(P)).then_inc(bias_loaded, 16)
            for ch in range(2, NCH):
                sp.wait_ge(wx_hi_cut, ch - 1)
                sp.wait_ge(wx_lo_cut, ch - 1)
                for j in range(NJ):
                    sp.dma_start(wx_raw[L * j:L * j + L, ch % 2], wx_view[ch, j]).then_inc(wx_loaded[ch % 2], 16)
            for n in range(LEAD):
                sp.wait_ge(x_turned, n + 1)
                load_x(n + 2, n)
            load_res(0, 0)
            for n in range(LEAD):
                sp.wait_ge(proj_staged, NJ * (n + 1))
                place_xw(n)

            def block(i, n, r, has):
                if has(4):
                    sp.wait_ge(x_turned, n + 3)
                    load_x(n + 4, r)
                if has(1):
                    if started(n):
                        sp.wait_ge(y_done, n * TB)
                    load_res(n + 1, 1 - r)
                if has(LEAD):
                    sp.wait_ge(proj_staged, n * NJ + NJ * (LEAD + 1))
                    place_xw(r)
                sp.wait_ge(y_done, n * TB + TB)
                for j in range(NJ):
                    sp.dma_start(out_view[j, :, bass.ds(n * TB, TB), :], y[L * j:L * j + B, r]).then_inc(y_stored[r], 16)

            run_blocks(sp, block)
            for r in range(2):
                sp.wait_ge(y_stored[r], 16 * NJ * (NB // 2))

        @block_ctx.tensor
        def _(pe):
            def project(q, bankq, r, j, first):
                if first is not None:
                    pe.wait_ge(x_hi_cut, first)
                    pe.wait_ge(x_lo_cut, first)
                if started(q - 1):
                    pe.wait_ge(proj_staged, q - 1)
                cols = slice(j * ZW, (j + 1) * ZW)
                for ch in range(NCH):
                    for k, (xp, wp) in enumerate(((x_hi, wx_hi), (x_hi, wx_lo), (x_lo, wx_hi))):
                        mm = nc.tensor.matmul(PS[bankq][:, :], xp[:, r, ch, :], wp[:, ch, cols],
                                              start=(ch == 0 and k == 0), stop=(ch == NCH - 1 and k == 2))
                mm.then_inc(proj_done, 1)

            pe.wait_ge(h0_turned, 1)
            for ch in range(NCH):
                pe.wait_ge(wh_loaded[ch], 16 * NJ)
                raw = by_tile(wh_raw[:, ch])
                for j in range(NJ):
                    mm = nc.tensor.matmul(Z[L * j:L * j + B, :], h0_T[:, ch, :], raw[:, j],
                                          start=(ch == 0), stop=(ch == NCH - 1))
            mm.then_inc(z_done, 1)
            pe.wait_ge(wx_hi_cut, NCH)
            pe.wait_ge(wx_lo_cut, NCH)
            for n in range(LEAD):
                for j in range(NJ):
                    project(n * NJ + j, j % 2, n, j, n + 1 if j == 0 else None)

            def recurrent(t):
                for part, (ht, ready) in enumerate(((hT_hi, hT_hi_done), (hT_lo, hT_lo_done))):
                    pe.wait_ge(ready, t)
                    for ch in range(NCH):
                        ws = (wh_hi, wh_lo) if part == 0 else (wh_hi,)
                        for k, w in enumerate(ws):
                            for j in range(NJ):
                                mm = nc.tensor.matmul(Z[L * j:L * j + B, :], ht[:, ch, :], w[:, ch, j * ZW:(j + 1) * ZW],
                                                      start=(part == 0 and ch == 0 and k == 0),
                                                      stop=(part == 1 and ch == NCH - 1))
                mm.then_inc(z_done, 1)

            def block(i, n, r, has):
                for s in range(TB):
                    t = n * TB + s
                    if isinstance(t, int) and t == 1:
                        pe.wait_ge(wh_hi_cut, NCH)
                        pe.wait_ge(wh_lo_cut, NCH)
                    if started(t):
                        recurrent(t)
                    if has(LEAD):
                        project(n * NJ + LEAD * NJ + s, s % 2, r, s, n + LEAD + 1 if s == 0 else None)

            run_blocks(pe, block)

        @block_ctx.scalar
        def _(sc):
            def cut_x_hi(n, r, busy):
                sc.wait_ge(x_turned, n + 1)
                if busy is not None:
                    sc.wait_ge(proj_done, busy)
                nc.scalar.copy(x_hi[:, r], x_T[:, :, :, :].rearrange("p ch t b -> p ch (t b)")).then_inc(x_hi_cut, 1)

            cut_x_hi(0, 0, None)
            for ch in range(NCH):
                sc.wait_ge(wx_loaded[ch % 2], 16 * NJ * (ch // 2 + 1))
                nc.scalar.copy(as_tiles(wx_hi[:, ch]), by_tile(wx_raw[:, ch % 2])).then_inc(wx_hi_cut, 1)
            sc.wait_ge(scales_done, 2)
            for ch in range(NCH):
                nc.scalar.activation(as_tiles(wh_hi[:, ch]), by_tile(wh_raw[:, ch]), ACT.Copy,
                                     scale=w_scale[:, :].bitcast(F32)).then_inc(wh_hi_cut, 1)
            cut_x_hi(1, 1, None)
            cut_x_hi(2, 0, NJ)

            def block(i, n, r, has):
                for s in range(TB):
                    t = n * TB + s
                    sc.wait_ge(zx_if_done, t + 1)
                    nc.scalar.activation(act[:, IF], zx[:, IF], ACT.Sigmoid).then_inc(sig_if_done, 1)
                    sc.wait_ge(zx_g_done, t + 1)
                    nc.scalar.activation(act[:, Gt], zx[:, Gt], ACT.Tanh).then_inc(tanh_g_done, 1)
                    sc.wait_ge(zx_o_done, t + 1)
                    nc.scalar.activation(act[:, O], zx[:, O], ACT.Sigmoid).then_inc(sig_o_done, 1)
                    sc.wait_ge(c_done, t + 1)
                    nc.scalar.activation(tanh_c[:, :], c[:, :], ACT.Tanh).then_inc(tanh_c_done, 1)
                    if has(3) and s == 1:
                        cut_x_hi(n + 3, 1 - r, n * NJ + 2 * NJ)

            run_blocks(sc, block)

        @block_ctx.vector
        def _(v):
            def turn_x(n, r, count):
                v.wait_ge(x_loaded[r], 16 * NJ * count)
                if started(n):
                    v.wait_ge(x_hi_cut, n)
                    v.wait_ge(x_lo_cut, n)
                nc.vector.transpose(x_T[:, :, :, :].rearrange("p ch t b -> p t ch b"),
                                    x_in[:, r].rearrange("p t (ch l) -> p t ch l", ch=NCH)).then_inc(x_turned, 1)

            def stage_projection(q, bankq, r, j, before):
                v.wait_ge(proj_done, q + 1)
                if before is not None:
                    v.wait_ge(xw_placed[r], before)
                nc.vector.tensor_tensor(stage[:, r, j], PS[bankq][:, :], bias_tiles[:, j], ALU.add).then_inc(proj_staged, 1)

            bias_tiles = bias_bc[:, :].rearrange("p (g j c) -> p j g c", g=4, j=NJ)

            nc.vector.memset(c[:, :], 0.0).then_inc(c_cleared, 1)
            v.wait_ge(h0_loaded, 16 * NJ)
            nc.vector.transpose(h0_T[:, :, :], h0_in[:, :].rearrange("p (ch l) -> p ch l", ch=NCH)).then_inc(h0_turned, 1)
            turn_x(0, 0, 1)
            for ch in range(NCH):
                v.wait_ge(wh_loaded[ch], 16 * NJ)
                nc.vector.tensor_reduce(wmax4[:, ch:ch + 1], wh_raw[:, ch], AX.X, ALU.max,
                                        apply_absolute_value=True).then_inc(wmax4_done, 1)
            v.wait_ge(wmax4_done, NCH)
            nc.vector.tensor_reduce(wmax[:, :], wmax4[:, :], AX.X, ALU.max).then_inc(wmax_done, 1)
            for ch in range(NCH):
                v.wait_ge(wx_hi_cut, ch + 1)
                nc.vector.tensor_tensor(as_tiles(wx_lo[:, ch]), by_tile(wx_raw[:, ch % 2]),
                                        as_tiles(wx_hi[:, ch]).bitcast(F32), ALU.subtract).then_inc(wx_lo_cut, 1)
            v.wait_ge(wmax_shared, 1)
            nc.vector.tensor_scalar(field[:, :], wmax_all[:, :].bitcast(I32), 255 << MANT, None,
                                    ALU.bitwise_and).then_inc(scale_step, 1)
            v.wait_ge(scale_step, 1)
            nc.vector.tensor_scalar(field2[:, :], field[:, :], float(MIN_FIELD << MANT), None, ALU.max).then_inc(scale_step, 1)
            v.wait_ge(scale_step, 2)
            nc.vector.tensor_scalar(w_scale[:, :], field2[:, :], -1.0, float((2 * EXP_ONE + W_TOP) << MANT),
                                    ALU.mult, ALU.add).then_inc(scales_done, 1)
            nc.vector.tensor_scalar(z_scale[:, :], field2[:, :], float(-(W_TOP + H_SCALE_LOG2) * 2 ** MANT), None,
                                    ALU.add).then_inc(scales_done, 1)
            v.wait_ge(scales_done, 2)
            for ch in range(NCH):
                v.wait_ge(wh_hi_cut, ch + 1)
                for j in range(NJ):
                    cut = nc.vector.scalar_tensor_tensor(as_tiles(wh_lo[:, ch])[:, j], by_tile(wh_raw[:, ch])[:, j],
                                                         w_scale[:, :].bitcast(F32), as_tiles(wh_hi[:, ch])[:, j],
                                                         ALU.mult, ALU.subtract)
                cut.then_inc(wh_lo_cut, 1)
            turn_x(1, 1, 1)
            v.wait_ge(bias_loaded, 16)
            v.wait_ge(z_done, 1)
            v.wait_ge(wh_lo_cut, NCH)
            for q in range(LEAD * NJ):
                stage_projection(q, q % 2, q // NJ, q % NJ, None)
                if q == NJ - 1:
                    turn_x(2, 0, 2)
            v.wait_ge(c_cleared, 1)

            def step(t, s, r, xw_count):
                first = isinstance(t, int) and t == 0
                v.wait_ge(z_done, t + 1)
                if s == 0:
                    v.wait_ge(xw_placed[r], xw_count)
                scale = 1.0 if first else z_scale[:, :].bitcast(F32)
                for cols, done in ((IF, zx_if_done), (Gt, zx_g_done), (O, zx_o_done)):
                    nc.vector.scalar_tensor_tensor(zx[:, cols], Z[:, cols], scale, xw[:, r, s, cols],
                                                   ALU.mult, ALU.add).then_inc(done, 1)
                v.wait_ge(sig_if_done, t + 1)
                nc.vector.tensor_tensor(fc[:, :], act[:, F], c[:, :], ALU.mult).then_inc(fc_done, 1)
                v.wait_ge(tanh_g_done, t + 1)
                nc.vector.tensor_tensor(ig[:, :], act[:, I], act[:, Gt], ALU.mult).then_inc(ig_done, 1)
                v.wait_ge(fc_done, t + 1)
                v.wait_ge(ig_done, t + 1)
                nc.vector.tensor_tensor(c[:, :], fc[:, :], ig[:, :], ALU.add).then_inc(c_done, 1)
                v.wait_ge(sig_o_done, t + 1)
                v.wait_ge(tanh_c_done, t + 1)
                nc.vector.scalar_tensor_tensor(h_hi[:, :], act[:, O], H_SCALE, tanh_c[:, :],
                                               ALU.mult, ALU.mult).then_inc(h_hi_done, 1)
                v.wait_ge(h_hi_done, t + 1)
                nc.vector.transpose(hT_hi[:, :, :], h_hi[:, :].rearrange("p (ch l) -> p ch l", ch=NCH)).then_inc(hT_hi_done, 1)
                if started(t - 1):
                    v.wait_ge(y_done, t - 1)
                nc.vector.tensor_tensor(h32[:, s % 2], act[:, O], tanh_c[:, :], ALU.mult).then_inc(h32_done, 1)
                v.wait_ge(h32_done, t + 1)
                nc.vector.scalar_tensor_tensor(h_lo[:, :], h32[:, s % 2], H_SCALE, h_hi[:, :],
                                               ALU.mult, ALU.subtract).then_inc(h_lo_done, 1)
                v.wait_ge(h_lo_done, t + 1)
                nc.vector.transpose(hT_lo[:, :, :], h_lo[:, :].rearrange("p (ch l) -> p ch l", ch=NCH)).then_inc(hT_lo_done, 1)

            def block(i, n, r, has):
                placed = (i + 1) * (16 * NJ * TB)
                for s in range(TB):
                    step(n * TB + s, s, r, placed)
                    if has(LEAD):
                        stage_projection(n * NJ + LEAD * NJ + s, s % 2, r, s, placed if s == 0 else None)
                    if has(3) and s == 1:
                        turn_x(n + 3, 1 - r, i + 2 + r)

            run_blocks(v, block)

        @block_ctx.gpsimd
        def _(pool):
            def cut_x_lo(n, r):
                pool.wait_ge(x_hi_cut, n + 1)
                nc.gpsimd.tensor_tensor(x_lo[:, r], x_T[:, :, :, :].rearrange("p ch t b -> p ch (t b)"),
                                        x_hi[:, r].bitcast(F32), ALU.subtract).then_inc(x_lo_cut, 1)

            cut_x_lo(0, 0)
            pool.wait_ge(wmax_done, 1)
            nc.gpsimd.partition_all_reduce(wmax_all[:, :], wmax[:, :], P, bass.bass_isa.ReduceOp.max).then_inc(wmax_shared, 1)
            cut_x_lo(1, 1)
            cut_x_lo(2, 0)

            def block(i, n, r, has):
                for s in range(TB):
                    t = n * TB + s
                    pool.wait_ge(h32_done, t + 1)
                    if s == 0:
                        pool.wait_ge(res_loaded[r], (i + 1) * (16 * NJ))
                        if started(i):
                            pool.wait_ge(y_stored[r], i * (16 * NJ))
                    nc.gpsimd.tensor_tensor(y[:, r, s], h32[:, s % 2], x_res[:, r, s], ALU.add).then_inc(y_done, 1)
                    if has(3) and s == 1:
                        cut_x_lo(n + 3, 1 - r)

            run_blocks(pool, block)


def kernel(x, cond_1024, L0_cond_Wx, L0_cond_Wh, L0_cond_b):
    import concourse.bacc as bacc
    from concourse.bass_utils import run_bass_kernel_spmd

    nc = bacc.Bacc("TRN2", target_bir_lowering=False, num_devices=1)
    given = {"x": x, "h0": cond_1024, "Wx": L0_cond_Wx, "Wh": L0_cond_Wh, "bias": L0_cond_b}
    arrays = {f"in_{name}": np.ascontiguousarray(a) for name, a in given.items()}
    ins = [nc.dram_tensor(name, a.shape, mybir.dt.from_np(a.dtype), kind="ExternalInput").ap()
           for name, a in arrays.items()]
    y = nc.dram_tensor("out_y", arrays["in_x"].shape, F32, kind="ExternalOutput").ap()
    lstm_residual(nc, *ins, y)
    return run_bass_kernel_spmd(nc, [arrays], core_ids=[0]).results[0]["out_y"]
```

```python
from contextlib import ExitStack

import numpy as np
import concourse.bass as bass
from concourse import mybir

F32 = mybir.dt.float32
F32R = mybir.dt.float32r
F16 = mybir.dt.float16
I32 = mybir.dt.int32
ALU = mybir.AluOpType
ACT = mybir.ActivationFunctionType
AX = mybir.AxisListType


def lstm_residual(nc, x, h0, Wx, Wh, bias, out):
    B, T, D = x.shape
    H = h0.shape[1]
    G = 4 * H
    P = 128
    NJ = H // P
    C = P
    NCH = D // P
    L = 32
    ZW = 4 * C
    TB = P // B
    NB = T // TB
    BODY = 2
    LEAD = 2
    H_SCALE_LOG2 = 12
    H_SCALE = float(2 ** H_SCALE_LOG2)
    EXP_ONE = 127
    W_TOP = 14
    MIN_FIELD = W_TOP + H_SCALE_LOG2 + 1
    MANT = 23

    ctx = ExitStack()
    with ctx:
        def sb(name, shape, dt=F32):
            return ctx.enter_context(nc.sbuf_tensor(name, shape, dt))

        def bank(name):
            return ctx.enter_context(nc.psum_tensor(name, [P, 512], F32))

        def sem(name):
            return ctx.enter_context(nc.semaphore(name))

        wx_hi = sb("wx_hi", [P, NCH, G], F32R)
        wx_lo = sb("wx_lo", [P, NCH, G], F32R)
        wh_hi = sb("wh_hi", [P, NCH, G], F16)
        wh_lo = sb("wh_lo", [P, NCH, G], F16)
        wx_raw = sb("wx_raw", [P, NCH, G])
        wh_raw = sb("wh_raw", [P, NCH, G])
        stage = wx_raw[:, 0:2].rearrange("p r (j n) -> p r j n", j=NJ)
        CUT_ORDER = (2, 3, 0, 1)
        xw = wh_raw[:, 2:4].rearrange("p r (t n) -> p r t n", t=TB)
        bias_bc = sb("bias_bc", [P, G])
        x_in = sb("x_in", [P, 2, TB, C])
        x_T = sb("x_T", [P, NCH, TB, B])
        x_hi = sb("x_hi", [P, 2, NCH, TB * B], F32R)
        x_lo = sb("x_lo", [P, 2, NCH, TB * B], F32R)
        x_res = sb("x_res", [P, 2, TB, C])
        y = sb("y", [P, 2, TB, C])
        h0_in = sb("h0_in", [P, C])
        h0_T = sb("h0_T", [P, NCH, B])
        zx = sb("zx", [P, ZW])
        act = sb("act", [P, ZW])
        fc = sb("fc", [P, C])
        ig = sb("ig", [P, C])
        c = sb("c", [P, C])
        tanh_c = sb("tanh_c", [P, C])
        h32 = sb("h32", [P, 2, C])
        h_hi = sb("h_hi", [P, C], F16)
        h_lo = sb("h_lo", [P, C], F16)
        hT_hi = sb("hT_hi", [P, NCH, B], F16)
        hT_lo = sb("hT_lo", [P, NCH, B], F16)
        wmax4 = sb("wmax4", [P, NCH])
        wmax = sb("wmax", [P, 1])
        wmax_all = sb("wmax_all", [P, 1])
        field = sb("field", [P, 1], I32)
        field2 = sb("field2", [P, 1], I32)
        w_scale = sb("w_scale", [P, 1], I32)
        z_scale = sb("z_scale", [P, 1], I32)

        Z = bank("Z")
        PS = [bank("PS0"), bank("PS1")]

        wx_loaded = [sem(f"wx_loaded{ch}") for ch in range(NCH)]
        wh_loaded = [sem(f"wh_loaded{ch}") for ch in range(NCH)]
        bias_loaded = sem("bias_loaded")
        h0_loaded = sem("h0_loaded")
        x_loaded = [sem("x_loaded0"), sem("x_loaded1")]
        res_loaded = [sem("res_loaded0"), sem("res_loaded1")]
        xw_placed = [[sem(f"xw_placed{r}_{t}") for t in range(TB)] for r in range(2)]
        y_stored = [sem("y_stored0"), sem("y_stored1")]
        wx_hi_cut = sem("wx_hi_cut")
        wx_lo_cut = sem("wx_lo_cut")
        wmax4_done = sem("wmax4_done")
        wmax_done = sem("wmax_done")
        wmax_shared = sem("wmax_shared")
        scale_step = sem("scale_step")
        scales_done = sem("scales_done")
        wh_hi_cut = sem("wh_hi_cut")
        wh_lo_cut = sem("wh_lo_cut")
        h0_turned = sem("h0_turned")
        c_cleared = sem("c_cleared")
        x_turned = sem("x_turned")
        x_hi_cut = sem("x_hi_cut")
        x_lo_cut = sem("x_lo_cut")
        proj_done = sem("proj_done")
        proj_staged = sem("proj_staged")
        z_done = sem("z_done")
        zx_done = sem("zx_done")
        sig_done = sem("sig_done")
        tanh_g_done = sem("tanh_g_done")
        ig_done = sem("ig_done")
        c_done = sem("c_done")
        tanh_c_done = sem("tanh_c_done")
        h_hi_done = sem("h_hi_done")
        hT_hi_done = sem("hT_hi_done")
        h32_done = sem("h32_done")
        h_lo_done = sem("h_lo_done")
        hT_lo_done = sem("hT_lo_done")
        y_done = sem("y_done")

        x_view = x.rearrange("b t (j c) -> j b t c", j=NJ)
        out_view = out.rearrange("b t (j c) -> j b t c", j=NJ)
        wx_view = Wx.rearrange("(j ch l) g -> ch j l g", j=NJ, ch=NCH)
        wh_view = Wh.rearrange("(j ch l) g -> ch j l g", j=NJ, ch=NCH)
        h0_view = h0.rearrange("b (j c) -> j b c", j=NJ)

        HC = C // 2

        def half(tile, a):
            return tile[:, a * HC:(a + 1) * HC]

        def half_gates(tile, a):
            return tile.rearrange("p (g a c) -> p a g c", g=4, a=2)[:, a]

        def by_tile(w):
            return w.rearrange("p (g j c) -> p j g c", g=4, j=NJ)

        def as_tiles(w):
            return w.rearrange("p (j g c) -> p j g c", g=4, j=NJ)

        def started(value):
            return not isinstance(value, int) or value > 0

        def run_blocks(engine, block):
            def body(i, static):
                for r in range(BODY):
                    n = i * BODY + r
                    block(i, n, r, (lambda k, n=n: n + k < NB) if static else (lambda k: True))
            last = NB // BODY
            body(0, True)
            with engine.Fori(1, last - 2) as i:
                body(i, False)
            body(last - 2, True)
            body(last - 1, True)

        block_ctx = ctx.enter_context(nc.Block())

        @block_ctx.sync
        def _(sp):
            def load_x(n, r):
                for j in range(NJ):
                    sp.dma_start(x_in[L * j:L * j + B, r], x_view[j, :, bass.ds(n * TB, TB), :]).then_inc(x_loaded[r], 16)

            def load_res(n, r):
                for j in range(NJ):
                    sp.dma_start(x_res[L * j:L * j + B, r], x_view[j, :, bass.ds(n * TB, TB), :]).then_inc(res_loaded[r], 16)

            def place_xw(r):
                for t in range(TB):
                    for j in range(NJ):
                        sp.dma_start(xw[L * j:L * j + B, r, t], stage[B * t:B * t + B, r, j]).then_inc(xw_placed[r][t], 16)

            for ch in range(NCH):
                for j in range(NJ):
                    sp.dma_start(wx_raw[L * j:L * j + L, ch], wx_view[ch, j]).then_inc(wx_loaded[ch], 16)
                if ch < LEAD:
                    load_x(ch, ch)
            sp.dma_start(bias_bc[:, :], bias.partition_broadcast(P)).then_inc(bias_loaded, 16)
            for j in range(NJ):
                sp.dma_start(h0_in[L * j:L * j + B], h0_view[j]).then_inc(h0_loaded, 16)
            for ch in range(NCH):
                for j in range(NJ):
                    sp.dma_start(wh_raw[L * j:L * j + L, ch], wh_view[ch, j]).then_inc(wh_loaded[ch], 16)
            for n in range(LEAD):
                sp.wait_ge(x_turned, n + 1)
                load_x(n + 2, n)
            load_res(0, 0)
            sp.wait_ge(z_done, 1)
            for n in range(LEAD):
                sp.wait_ge(wh_hi_cut, n + 1)
                sp.wait_ge(wh_lo_cut, n + 1)
                sp.wait_ge(proj_staged, NJ * (n + 1))
                place_xw(n)

            def block(i, n, r, has):
                if has(4):
                    sp.wait_ge(x_turned, n + 3)
                    load_x(n + 4, r)
                if has(1):
                    if started(n):
                        sp.wait_ge(y_done, n * TB)
                    load_res(n + 1, 1 - r)
                if has(LEAD):
                    sp.wait_ge(proj_staged, n * NJ + NJ * (LEAD + 1))
                    place_xw(r)
                sp.wait_ge(y_done, n * TB + TB)
                for j in range(NJ):
                    sp.dma_start(out_view[j, :, bass.ds(n * TB, TB), :], y[L * j:L * j + B, r]).then_inc(y_stored[r], 16)

            run_blocks(sp, block)
            for r in range(2):
                sp.wait_ge(y_stored[r], 16 * NJ * (NB // 2))

        @block_ctx.tensor
        def _(pe):
            def project(q, bankq, r, j, first):
                if first is not None:
                    pe.wait_ge(x_hi_cut, first)
                    pe.wait_ge(x_lo_cut, first)
                if started(q - 1):
                    pe.wait_ge(proj_staged, q - 1)
                cols = slice(j * ZW, (j + 1) * ZW)
                for ch in range(NCH):
                    if isinstance(q, int) and q == 0:
                        pe.wait_ge(wx_hi_cut, ch + 1)
                        pe.wait_ge(wx_lo_cut, ch + 1)
                    for k, (xp, wp) in enumerate(((x_hi, wx_hi), (x_hi, wx_lo), (x_lo, wx_hi))):
                        mm = nc.tensor.matmul(PS[bankq][:, :], xp[:, r, ch, :], wp[:, ch, cols],
                                              start=(ch == 0 and k == 0), stop=(ch == NCH - 1 and k == 2))
                mm.then_inc(proj_done, 1)

            def project_block(n):
                for j in range(NJ):
                    project(n * NJ + j, j % 2, n, j, n + 1 if j == 0 else None)

            project_block(0)
            pe.wait_ge(h0_turned, 1)
            for ch in range(NCH):
                pe.wait_ge(wh_loaded[ch], 16 * NJ)
                raw = by_tile(wh_raw[:, ch])
                for j in range(NJ):
                    mm = nc.tensor.matmul(Z[L * j:L * j + B, :], h0_T[:, ch, :], raw[:, j],
                                          start=(ch == 0), stop=(ch == NCH - 1))
            mm.then_inc(z_done, 1)
            project_block(1)

            def recurrent(t):
                for part, ht in enumerate((hT_hi, hT_lo)):
                    for ch in range(NCH):
                        if part == 0 and ch % 2 == 0:
                            pe.wait_ge(hT_hi_done, 2 * t - 1 + ch // 2)
                        if part == 1 and ch == 0:
                            pe.wait_ge(hT_lo_done, t)
                        ws = (wh_hi, wh_lo) if part == 0 else (wh_hi,)
                        for k, w in enumerate(ws):
                            for j in range(NJ):
                                mm = nc.tensor.matmul(Z[L * j:L * j + B, :], ht[:, ch, :], w[:, ch, j * ZW:(j + 1) * ZW],
                                                      start=(part == 0 and ch == 0 and k == 0),
                                                      stop=(part == 1 and ch == NCH - 1))
                mm.then_inc(z_done, 1)

            def block(i, n, r, has):
                for s in range(TB):
                    t = n * TB + s
                    if isinstance(t, int) and t == 1:
                        pe.wait_ge(wh_hi_cut, NCH)
                        pe.wait_ge(wh_lo_cut, NCH)
                    if started(t):
                        recurrent(t)
                    if has(LEAD):
                        project(n * NJ + LEAD * NJ + s, s % 2, r, s, n + LEAD + 1 if s == 0 else None)

            run_blocks(pe, block)

        @block_ctx.scalar
        def _(sc):
            def cut_x_hi(n, r, busy):
                sc.wait_ge(x_turned, n + 1)
                if busy is not None:
                    sc.wait_ge(proj_done, busy)
                nc.scalar.copy(x_hi[:, r], x_T[:, :, :, :].rearrange("p ch t b -> p ch (t b)")).then_inc(x_hi_cut, 1)

            cut_x_hi(0, 0, None)
            for ch in range(NCH):
                sc.wait_ge(wx_loaded[ch], 16 * NJ)
                nc.scalar.copy(as_tiles(wx_hi[:, ch]), by_tile(wx_raw[:, ch])).then_inc(wx_hi_cut, 1)
            cut_x_hi(1, 1, None)
            sc.wait_ge(scales_done, 2)
            for ch in CUT_ORDER:
                nc.scalar.activation(as_tiles(wh_hi[:, ch]), by_tile(wh_raw[:, ch]), ACT.Copy,
                                     scale=w_scale[:, :].bitcast(F32)).then_inc(wh_hi_cut, 1)
            cut_x_hi(2, 0, NJ)

            def block(i, n, r, has):
                for s in range(TB):
                    t = n * TB + s
                    for a in range(2):
                        sc.wait_ge(zx_done, 2 * t + 1 + a)
                        nc.scalar.activation(half_gates(act, a)[:, 0:3], half_gates(zx, a)[:, 0:3],
                                             ACT.Sigmoid).then_inc(sig_done, 1)
                        nc.scalar.activation(half_gates(act, a)[:, 3], half_gates(zx, a)[:, 3],
                                             ACT.Tanh).then_inc(tanh_g_done, 1)
                    for a in range(2):
                        sc.wait_ge(c_done, 2 * t + 1 + a)
                        nc.scalar.activation(half(tanh_c, a), half(c, a), ACT.Tanh).then_inc(tanh_c_done, 1)
                    if has(3) and s == 1:
                        cut_x_hi(n + 3, 1 - r, n * NJ + 2 * NJ)

            run_blocks(sc, block)

        @block_ctx.vector
        def _(v):
            def turn_x(n, r, count):
                v.wait_ge(x_loaded[r], 16 * NJ * count)
                if started(n):
                    v.wait_ge(x_hi_cut, n)
                    v.wait_ge(x_lo_cut, n)
                nc.vector.transpose(x_T[:, :, :, :].rearrange("p ch t b -> p t ch b"),
                                    x_in[:, r].rearrange("p t (ch l) -> p t ch l", ch=NCH)).then_inc(x_turned, 1)

            def stage_projection(q, bankq, r, j, before):
                v.wait_ge(proj_done, q + 1)
                if before is not None:
                    for t in range(TB):
                        v.wait_ge(xw_placed[r][t], before)
                nc.vector.tensor_tensor(stage[:, r, j], PS[bankq][:, :], bias_tiles[:, j], ALU.add).then_inc(proj_staged, 1)

            bias_tiles = bias_bc[:, :].rearrange("p (g j c) -> p j g c", g=4, j=NJ)

            def prepare():
                nc.vector.memset(c[:, :], 0.0).then_inc(c_cleared, 1)
                turn_x(0, 0, 1)
                for ch in range(NCH):
                    v.wait_ge(wx_hi_cut, ch + 1)
                    nc.vector.tensor_tensor(as_tiles(wx_lo[:, ch]), by_tile(wx_raw[:, ch]),
                                            as_tiles(wx_hi[:, ch]).bitcast(F32), ALU.subtract).then_inc(wx_lo_cut, 1)
                v.wait_ge(h0_loaded, 16 * NJ)
                nc.vector.transpose(h0_T[:, :, :], h0_in[:, :].rearrange("p (ch l) -> p ch l", ch=NCH)).then_inc(h0_turned, 1)
                turn_x(1, 1, 1)
                v.wait_ge(bias_loaded, 16)
                v.wait_ge(wx_lo_cut, NCH)
                for ch in range(NCH):
                    stage_projection(ch, ch % 2, 0, ch, None)
                    v.wait_ge(wh_loaded[ch], 16 * NJ)
                    nc.vector.tensor_reduce(wmax4[:, ch:ch + 1], wh_raw[:, ch], AX.X, ALU.max,
                                            apply_absolute_value=True).then_inc(wmax4_done, 1)
                v.wait_ge(wmax4_done, NCH)
                nc.vector.tensor_reduce(wmax[:, :], wmax4[:, :], AX.X, ALU.max).then_inc(wmax_done, 1)
                v.wait_ge(wmax_shared, 1)
                nc.vector.tensor_scalar(field[:, :], wmax_all[:, :].bitcast(I32), 255 << MANT, None,
                                        ALU.bitwise_and).then_inc(scale_step, 1)
                v.wait_ge(scale_step, 1)
                nc.vector.tensor_scalar(field2[:, :], field[:, :], float(MIN_FIELD << MANT), None, ALU.max).then_inc(scale_step, 1)
                v.wait_ge(scale_step, 2)
                nc.vector.tensor_scalar(w_scale[:, :], field2[:, :], -1.0, float((2 * EXP_ONE + W_TOP) << MANT),
                                        ALU.mult, ALU.add).then_inc(scales_done, 1)
                nc.vector.tensor_scalar(z_scale[:, :], field2[:, :], float(-(W_TOP + H_SCALE_LOG2) * 2 ** MANT), None,
                                        ALU.add).then_inc(scales_done, 1)
                v.wait_ge(scales_done, 2)
                for k, ch in enumerate(CUT_ORDER):
                    v.wait_ge(wh_hi_cut, k + 1)
                    for j in range(NJ):
                        cut = nc.vector.scalar_tensor_tensor(as_tiles(wh_lo[:, ch])[:, j], by_tile(wh_raw[:, ch])[:, j],
                                                             w_scale[:, :].bitcast(F32), as_tiles(wh_hi[:, ch])[:, j],
                                                             ALU.mult, ALU.subtract)
                    cut.then_inc(wh_lo_cut, 1)
                    if k in (1, 2):
                        stage_projection(NJ + k - 1, k - 1, 1, k - 1, None)
                turn_x(2, 0, 2)

            def high_part_of_h(t, a):
                v.wait_ge(tanh_c_done, 2 * t + 1 + a)
                nc.vector.scalar_tensor_tensor(half(h_hi, a), half_gates(act, a)[:, 2], H_SCALE, half(tanh_c, a),
                                               ALU.mult, ALU.mult).then_inc(h_hi_done, 1)

            def turn_high_part(t, a):
                v.wait_ge(h_hi_done, 2 * t + 1 + a)
                nc.vector.transpose(hT_hi[:, NCH // 2 * a:NCH // 2 * (a + 1), :],
                                    half(h_hi, a).rearrange("p (ch l) -> p ch l", l=L)).then_inc(hT_hi_done, 1)

            def step(t, s, r, xw_count):
                first = isinstance(t, int) and t == 0
                v.wait_ge(xw_placed[r][s], xw_count)
                v.wait_ge(z_done, t + 1)
                scale = 1.0 if first else z_scale[:, :].bitcast(F32)
                for a in range(2):
                    nc.vector.scalar_tensor_tensor(half_gates(zx, a), half_gates(Z, a), scale,
                                                   half_gates(xw[:, r, s], a), ALU.mult, ALU.add).then_inc(zx_done, 1)
                v.wait_ge(sig_done, 2 * t + 1)
                nc.vector.tensor_tensor(half(fc, 0), half_gates(act, 0)[:, 1], half(c, 0), ALU.mult)
                v.wait_ge(tanh_g_done, 2 * t + 1)
                nc.vector.tensor_tensor(half(ig, 0), half_gates(act, 0)[:, 0], half_gates(act, 0)[:, 3], ALU.mult).then_inc(ig_done, 1)
                v.wait_ge(ig_done, 2 * t + 1)
                nc.vector.tensor_tensor(half(c, 0), half(fc, 0), half(ig, 0), ALU.add).then_inc(c_done, 1)
                v.wait_ge(sig_done, 2 * t + 2)
                nc.vector.tensor_tensor(half(fc, 1), half_gates(act, 1)[:, 1], half(c, 1), ALU.mult)
                v.wait_ge(tanh_g_done, 2 * t + 2)
                nc.vector.tensor_tensor(half(ig, 1), half_gates(act, 1)[:, 0], half_gates(act, 1)[:, 3], ALU.mult).then_inc(ig_done, 1)
                high_part_of_h(t, 0)
                v.wait_ge(ig_done, 2 * t + 2)
                nc.vector.tensor_tensor(half(c, 1), half(fc, 1), half(ig, 1), ALU.add).then_inc(c_done, 1)
                turn_high_part(t, 0)
                high_part_of_h(t, 1)
                turn_high_part(t, 1)
                if started(t - 1):
                    v.wait_ge(y_done, t - 1)
                nc.vector.tensor_tensor(h32[:, s % 2], act[:, 2 * C:3 * C], tanh_c[:, :], ALU.mult).then_inc(h32_done, 1)
                v.wait_ge(h32_done, t + 1)
                nc.vector.scalar_tensor_tensor(h_lo[:, :], h32[:, s % 2], H_SCALE, h_hi[:, :],
                                               ALU.mult, ALU.subtract).then_inc(h_lo_done, 1)
                v.wait_ge(h_lo_done, t + 1)
                nc.vector.transpose(hT_lo[:, :, :], h_lo[:, :].rearrange("p (ch l) -> p ch l", ch=NCH)).then_inc(hT_lo_done, 1)

            def block(i, n, r, has):
                placed = (i + 1) * (16 * NJ)
                for s in range(TB):
                    if started(n * TB + s):
                        step(n * TB + s, s, r, placed)
                    if has(LEAD):
                        stage_projection(n * NJ + LEAD * NJ + s, s % 2, r, s, placed if s == 0 else None)
                    if has(3) and s == 1:
                        turn_x(n + 3, 1 - r, i + 2 + r)

            prepare()
            v.wait_ge(c_cleared, 1)
            step(0, 0, 0, 16 * NJ)
            for j in range(2, NJ):
                stage_projection(NJ + j, j % 2, 1, j, None)
            run_blocks(v, block)

        @block_ctx.gpsimd
        def _(pool):
            def cut_x_lo(n, r):
                pool.wait_ge(x_hi_cut, n + 1)
                nc.gpsimd.tensor_tensor(x_lo[:, r], x_T[:, :, :, :].rearrange("p ch t b -> p ch (t b)"),
                                        x_hi[:, r].bitcast(F32), ALU.subtract).then_inc(x_lo_cut, 1)

            cut_x_lo(0, 0)
            pool.wait_ge(wmax_done, 1)
            nc.gpsimd.partition_all_reduce(wmax_all[:, :], wmax[:, :], P, bass.bass_isa.ReduceOp.max).then_inc(wmax_shared, 1)
            cut_x_lo(1, 1)
            cut_x_lo(2, 0)

            def block(i, n, r, has):
                for s in range(TB):
                    t = n * TB + s
                    pool.wait_ge(h32_done, t + 1)
                    if s == 0:
                        pool.wait_ge(res_loaded[r], (i + 1) * (16 * NJ))
                        if started(i):
                            pool.wait_ge(y_stored[r], i * (16 * NJ))
                    nc.gpsimd.tensor_tensor(y[:, r, s], h32[:, s % 2], x_res[:, r, s], ALU.add).then_inc(y_done, 1)
                    if has(3) and s == 1:
                        cut_x_lo(n + 3, 1 - r)

            run_blocks(pool, block)


def kernel(x, cond_1024, L0_cond_Wx, L0_cond_Wh, L0_cond_b):
    import concourse.bacc as bacc
    from concourse.bass_utils import run_bass_kernel_spmd

    nc = bacc.Bacc("TRN2", target_bir_lowering=False, num_devices=1)
    given = {"x": x, "h0": cond_1024, "Wx": L0_cond_Wx, "Wh": L0_cond_Wh, "bias": L0_cond_b}
    arrays = {f"in_{name}": np.ascontiguousarray(a) for name, a in given.items()}
    ins = [nc.dram_tensor(name, a.shape, mybir.dt.from_np(a.dtype), kind="ExternalInput").ap()
           for name, a in arrays.items()]
    y = nc.dram_tensor("out_y", arrays["in_x"].shape, F32, kind="ExternalOutput").ap()
    lstm_residual(nc, *ins, y)
    return run_bass_kernel_spmd(nc, [arrays], core_ids=[0]).results[0]["out_y"]
```
